# Optimizing a Trainium2 kernel written in Bass

```python
import numpy as np
import jax
import jax.numpy as jnp

def _softmax(x, axis=-1):
    return jax.nn.softmax(x, axis=axis)

def _gelu(x):
    return jax.nn.gelu(x, approximate=True)

def _silu(x):
    return jax.nn.silu(x)

def _sigmoid(x):
    return jax.nn.sigmoid(x)

def _layernorm(x, axis=-1, eps=1e-05):
    m = jnp.mean(x, axis=axis, keepdims=True)
    v = jnp.var(x, axis=axis, keepdims=True)
    return (x - m) / jnp.sqrt(v + eps)

def _scatter_add(tgt, idx, src, axis=0):
    return tgt.at[idx].add(src)

def _segment_sum(src, seg, n):
    return jax.ops.segment_sum(src, seg, n)
kernel_name = 'mk_gnn_preln_d2_gnn_r32_b4cbd6'

def setup_inputs(seed: int=0):
    np.random.seed(seed)
    _w = jnp.asarray

    def _rec_inputs():
        import jax
        import jax.numpy as jnp
        _gk = jax.random.key(seed)
        x = -0.0003713 + 1 * jax.random.normal(jax.random.fold_in(_gk, 1), (50000, 256), jnp.float32)
        src = jax.random.randint(jax.random.fold_in(_gk, 2), (50000,), 0, 50000, jnp.int32)
        dst = jax.random.randint(jax.random.fold_in(_gk, 3), (50000,), 0, 50000, jnp.int32)
        _o = jnp.argsort(dst, stable=True)
        src = src[_o]
        dst = dst[_o]
        edge_type_8 = jax.random.randint(jax.random.fold_in(_gk, 13), (50000,), 0, 8, jnp.int32)
        return (x, src, dst, edge_type_8)
    x, src, dst, edge_type_8 = _rec_inputs()

    def _L0_gnn_setup():
        import jax, jax.numpy as jnp
        import numpy as np
        N_NODES = 50000
        N_EDGES = 25000
        D_IN = 256
        D_OUT = 256
        N_REL = 8
        key = jax.random.key(seed)
        k_x, k_ei, k_et, k_w = jax.random.split(key, 4)
        x = jax.random.normal(k_x, (N_NODES, D_IN), dtype=jnp.float32)
        edge_index = jax.random.randint(k_ei, (2, N_EDGES), 0, N_NODES, dtype=jnp.int32)
        edge_type = jax.random.randint(k_et, (N_EDGES,), 0, N_REL, dtype=jnp.int32)
        limit = float(np.sqrt(6.0 / (D_IN + D_OUT)))
        weight = jax.random.uniform(k_w, (N_REL, D_IN, D_OUT), dtype=jnp.float32, minval=-limit, maxval=limit)
        bias = jnp.zeros((D_OUT,), dtype=jnp.float32)
        return {'x': x, 'edge_index': edge_index, 'edge_type': edge_type, 'weight': weight, 'bias': bias}
    _L0_gnn_all = _L0_gnn_setup()
    _L0_gnn_in = {k: v for k, v in _L0_gnn_all.items() if k in ('weight', 'bias')}
    del _L0_gnn_all

    def _L1_gnn_setup():
        import jax, jax.numpy as jnp
        import numpy as np
        N = 3125
        E = 50000
        IN_FEATS = 256
        OUT_FEATS = 256
        MAXK = 32

        def _maxk(x, k):
            _, idx = jax.lax.top_k(x, k)
            rows = jnp.arange(x.shape[0])[:, None]
            mask = jnp.zeros_like(x).at[rows, idx].set(1.0)
            return x * mask
        key = jax.random.key(seed)
        k1, k2, k3, k4, k5 = jax.random.split(key, 5)
        feat = jax.random.normal(k1, (N, IN_FEATS), dtype=jnp.float32)
        W_self = jax.random.normal(k2, (IN_FEATS, OUT_FEATS), dtype=jnp.float32) * (1.0 / np.sqrt(IN_FEATS))
        W_neigh = jax.random.normal(k3, (IN_FEATS, OUT_FEATS), dtype=jnp.float32) * (1.0 / np.sqrt(IN_FEATS))
        src = jax.random.randint(k4, (E,), 0, N, dtype=jnp.int64)
        dst = jax.random.randint(k5, (E,), 0, N, dtype=jnp.int64)
        return {'feat': feat, 'W_self': W_self, 'W_neigh': W_neigh, 'src': src, 'dst': dst}
    _L1_gnn_all = _L1_gnn_setup()
    _L1_gnn_in = {k: v for k, v in _L1_gnn_all.items() if k in ('W_self', 'W_neigh')}
    del _L1_gnn_all
    return {'x': x, 'src': src, 'dst': dst, 'edge_type_8': edge_type_8, 'L0_gnn_weight': _L0_gnn_in['weight'], 'L0_gnn_bias': _L0_gnn_in['bias'], 'L1_gnn_W_self': _L1_gnn_in['W_self'], 'L1_gnn_W_neigh': _L1_gnn_in['W_neigh']}

def reference(x, src, dst, edge_type_8, L0_gnn_weight, L0_gnn_bias, L1_gnn_W_self, L1_gnn_W_neigh):
    import jax
    import jax.numpy as jnp

    def _L0_gnn_ref(x, edge_index, edge_type, weight, bias):
        import jax, jax.numpy as jnp
        import numpy as np
        N_NODES = 50000
        N_EDGES = 25000
        D_IN = 256
        D_OUT = 256
        N_REL = 8
        num_nodes = x.shape[0]
        row, col = (edge_index[0], edge_index[1])
        xt = jnp.einsum('ni,rio->rno', x, weight)
        messages = xt[edge_type, col]
        out = jax.ops.segment_sum(messages, row, num_segments=num_nodes)
        return jax.nn.relu(out + bias)

    def _L1_gnn_ref(feat, W_self, W_neigh, src, dst):
        import jax, jax.numpy as jnp
        import numpy as np
        N = 3125
        E = 50000
        IN_FEATS = 256
        OUT_FEATS = 256
        MAXK = 32

        def _maxk(x, k):
            _, idx = jax.lax.top_k(x, k)
            rows = jnp.arange(x.shape[0])[:, None]
            mask = jnp.zeros_like(x).at[rows, idx].set(1.0)
            return x * mask
        n = feat.shape[0]
        h_self = feat @ W_self
        h_neigh = feat @ W_neigh
        h_sparse = _maxk(h_neigh, MAXK)
        msg = h_sparse[src]
        summed = jax.ops.segment_sum(msg, dst, num_segments=n)
        deg = jax.ops.segment_sum(jnp.ones((src.shape[0],), dtype=feat.dtype), dst, num_segments=n)
        neigh = summed / jnp.maximum(deg, 1.0)[:, None]
        return h_self + neigh
    edge_index = jnp.stack([src, dst])
    h = jnp.maximum(_layernorm(x, axis=-1), 0.0)
    x = x + _L0_gnn_ref(h, edge_index, edge_type_8, L0_gnn_weight, L0_gnn_bias)
    h = jnp.maximum(_layernorm(x, axis=-1), 0.0)
    x = x + _L1_gnn_ref(h, L1_gnn_W_self, L1_gnn_W_neigh, src, dst)
    return x

_drawn_inputs = setup_inputs


def setup_inputs(seed=0):
    import zlib

    import numpy as np

    out = dict(_drawn_inputs(seed))
    spreads = {'L0_gnn_bias': (0.0, 0.1)}
    factors = {}
    for name, (base, spread) in spreads.items():
        noise = np.random.default_rng([zlib.crc32(name.encode()), seed]).standard_normal(out[name].shape)
        drawn = base * np.exp(spread * noise) if base else spread * noise
        out[name] = jnp.asarray(drawn.astype(out[name].dtype))
    for name, factor in factors.items():
        out[name] = (out[name] * factor).astype(out[name].dtype)
    return out
```

```python
import concourse.bass as bass
from concourse import mybir
from contextlib import ExitStack

F32 = mybir.dt.float32
F16 = mybir.dt.float16
I32 = mybir.dt.int32
ALU = mybir.AluOpType
ACT = mybir.ActivationFunctionType

P = 128
D = 256
KC = D // P
N = 50000
NE = 50000
R = 8
TOPK = 32
B = 4
BE = B * P
TILES = 392
NB = TILES // B
NBT = 106
SLOTS = NBT * B
COLS = 512
NPAD = TILES * P
SPARE = NPAD
ROWS = NPAD + BE
LOW = 2048
LOWBITS = 11
EPS = 1e-5
NEG = -3.0e38

assert TILES * P >= N and (NE + R * (BE - 1)) // BE <= NBT and NB % 2 == 0 and NBT % 2 == 0


def pipeline(eng, nb, lag, head, tail):
    first, last = 2 + lag, nb - 3 + lag % 2

    def step(i, c):
        for part, t in ((head, c), (tail, c - lag)):
            if i is not None:
                part(i * 2 + t, i + t // 2, t % 2)
            elif 0 <= t < nb:
                part(t, t // 2, t % 2)

    for t in range(first):
        step(None, t)
    with eng.Fori(0, (last + 1 - first) // 2) as i:
        step(i, first)
        step(i, first + 1)
    for t in range(last + 1, nb + lag):
        step(None, t)


def wait_from(eng, sem, value, batch, first):
    if not isinstance(batch, int) or batch >= first:
        eng.wait_ge(sem, value)


class Steps:

    def __init__(self, sem, per):
        self.sem, self.per = sem, per

    def start(self, batch):
        self.base, self.k = batch * self.per, 0

    def mark(self, ins):
        ins.then_inc(self.sem, 1)
        self.k += 1
        assert self.k <= self.per
        return self.base + self.k


def graph_layers(nc, x, src, dst, etype, w_rel, bias, w_self, w_neigh, out):
    agg = nc.dram_tensor("agg", [ROWS, D], F32).ap()
    hs = nc.dram_tensor("hs", [NPAD, D], F32).ap()
    key0_rows = nc.dram_tensor("key0_rows", [SLOTS * P], F32).ap()
    key1_rows = nc.dram_tensor("key1_rows", [NPAD], F32).ap()
    low1_rows = nc.dram_tensor("low1_rows", [NPAD], F32).ap()

    ctx = ExitStack()
    with ctx:
        def sb(name, shape, dt=F32):
            return ctx.enter_context(nc.sbuf_tensor(name, shape, dt))

        def sem(name):
            return ctx.enter_context(nc.semaphore(name))

        def pair(name):
            return [sem(f"{name}_even"), sem(f"{name}_odd")]

        bank = [ctx.enter_context(nc.psum_tensor(f"bank{i}", [P, 512], F32)) for i in range(8)]

        iota_i = sb("iota_i", [P, COLS], I32)
        iota_f = sb("iota_f", [P, COLS])
        iota_h = sb("iota_h", [P, COLS], F16)
        part_i = sb("part_i", [P, 1], I32)
        part_f = sb("part_f", [P, 1])
        spare_i = sb("spare_i", [P, B], I32)
        spare_f = sb("spare_f", [P, B])
        ident = sb("ident", [P, P])
        ones = sb("ones", [P, COLS])
        before = sb("before", [P, P])
        upto = sb("upto", [P, BE])
        zeros = sb("zeros", [P, 4 * D])
        eps = sb("eps", [P, 1])
        bias_sb = sb("bias_sb", [P, D])
        w0 = sb("w0", [P, R, KC, D])
        w1 = sb("w1", [P, KC, 2 * D])

        NAMES = ("type", "src", "dst")
        raw = {n: sb(f"raw_{n}", [P, COLS // P, P], I32) for n in NAMES}
        rawf = {n: sb(f"rawf_{n}", [P, COLS // P, P]) for n in NAMES}
        tab = {n: sb(f"tab_{n}", [P, COLS]) for n in NAMES}
        lowrow = sb("lowrow", [P, COLS // P, P])
        src_i = sb("src_i", [P, COLS], I32)
        dst_i = sb("dst_i", [P, COLS], I32)
        tmp_i = sb("tmp_i", [P, COLS], I32)
        tmp_f = sb("tmp_f", [P, COLS])
        val = [sb(f"val{k}", [P, COLS]) for k in range(3)]
        slot_tile = sb("slot_tile", [P, COLS])
        slot_row = sb("slot_row", [P, COLS])
        node_low = sb("node_low", [P, COLS])
        node_high = sb("node_high", [P, COLS])
        scan = sb("scan", [P, R, TILES])
        mask = sb("mask", [P, TILES])
        pos = sb("pos", [P, COLS])
        tot = sb("tot", [P, R])
        cnt_i = sb("cnt_i", [P, R], I32)
        nbat = sb("nbat", [P, R])
        incl = sb("incl", [P, R])
        off = sb("off", [P, R])
        btype_f = sb("btype_f", [1, P])
        btype = sb("btype", [1, P], I32)
        key0 = sb("key0", [P, COLS])
        from0 = sb("from0", [P, COLS], I32)
        deg_lo = sb("deg_lo", [P, TILES], F16)
        deg_hi = sb("deg_hi", [P, TILES], F16)
        one_tile = [sb(f"one_tile{p}", [P, SLOTS], F16) for p in range(2)]
        one_row = [sb(f"one_row{p}", [P, 3, P], F16) for p in range(2)]
        one_low = [sb(f"one_low{p}", [P, P], F16) for p in range(2)]
        one_high = [sb(f"one_high{p}", [P, TILES], F16) for p in range(2)]

        def two(name, shape, dt=F32):
            return [sb(f"{name}{p}", shape, dt) for p in range(2)]

        rows_in = two("rows_in", [P, B, D])
        h = two("h", [P, B, D])
        hT = two("hT", [P, KC, BE])
        msg = two("msg", [P, B * D])
        pick = [[sb(f"pick{p}{j}", [P, (j + 1) * P]) for j in range(B)] for p in range(2)]
        keyrow = two("keyrow", [P, BE])
        lowkey = two("lowkey", [P, BE])
        lowT = two("lowT", [P, BE], F16)
        gidx = two("gidx", [P, B], I32)
        sidx = two("sidx", [P, B], I32)
        keycol = two("keycol", [P, B])
        highcol = two("highcol", [P, B])
        seen = two("seen", [P, B])
        extra = two("extra", [P, B])
        stats = two("stats", [P, B, 6])
        mv = two("mv", [P, B, 2])
        std = two("std", [P, B])
        rstd = two("rstd", [P, B])
        shift = two("shift", [P, B])
        deg = two("deg", [P, B])
        agg_in = two("agg_in", [P, B, D])
        x2 = two("x2", [P, B, D])
        self_sb = two("self_sb", [P, B, D])
        neigh = two("neigh", [P, B, D])
        top = two("top", [P, B, D])
        work = sb("work", [P, B, D])
        best = sb("best", [P, B, 8])
        junk = scan

        consts = sem("consts")
        raw_in = sem("raw_in")
        weights_in = sem("weights_in")
        own = sem("own")
        dve_ready = sem("dve_ready")
        pe_done = sem("pe_done")
        rawf_done = sem("rawf_done")
        key1_stored = sem("key1_stored")
        hot = sem("hot")
        hot_used = sem("hot_used")
        keyT_done = sem("keyT_done")
        key0_stored = sem("key0_stored")
        btype_done = sem("btype_done")
        gathered0 = pair("gathered0")
        agg_zeroed = sem("agg_zeroed")
        added0 = pair("added0")
        keys0_in = pair("keys0_in")
        staged0 = sem("staged0")
        stats0 = sem("stats0")
        var0 = sem("var0")
        std0 = sem("std0")
        recip0 = sem("recip0")
        rstd0 = sem("rstd0")
        col0 = sem("col0")
        h0 = sem("h0")
        pick0 = sem("pick0")
        hTmm0 = sem("hTmm0")
        hT0 = sem("hT0")
        msgmm0 = sem("msgmm0")
        msg0 = sem("msg0")
        extra0 = sem("extra0")
        sidx0 = sem("sidx0")
        loaded = pair("loaded")
        pool_own = sem("pool_own")
        x2_done = sem("x2_done")
        stats_n = sem("stats_n")
        var_n = sem("var_n")
        std_n = sem("std_n")
        recip_n = sem("recip_n")
        rstd_n = sem("rstd_n")
        h_n = sem("h_n")
        hTtr = sem("hTtr")
        hT_n = sem("hT_n")
        mm_n = sem("mm_n")
        neigh_n = sem("neigh_n")
        self_n = sem("self_n")
        topk_own = sem("topk_own")
        top_n = sem("top_n")
        y_n = sem("y_n")
        y_stored = pair("y_stored")
        top_stored = pair("top_stored")
        spare_set = sem("spare_set")
        gathered1 = pair("gathered1")
        added1 = pair("added1")
        keys1_in = pair("keys1_in")
        staged1 = sem("staged1")
        col1 = sem("col1")
        pick1 = sem("pick1")
        degmm = sem("degmm")
        deg_own = sem("deg_own")
        rdeg1 = sem("rdeg1")
        foldmm = sem("foldmm")
        msg1 = sem("msg1")
        extra1 = sem("extra1")
        sidx1 = sem("sidx1")

        agg_halves = agg.rearrange("(s p r f) d -> s p r (f d)", s=2, p=P, f=2)

        passed = sem("passed")

        def wait_alone(eng, sem, value):
            eng.wait_ge(sem, value)
            eng.sem_inc(passed, 1)

        def edge0_over(eng):
            for q in range(2):
                eng.wait_ge(added0[q], 16 * B * (NBT // 2))

        def node_over(eng):
            for q in range(2):
                eng.wait_ge(y_stored[q], 16 * (NB // 2))
                eng.wait_ge(top_stored[q], 16 * (NB // 2))

        block = ctx.enter_context(nc.Block())

        @block.sync
        def _(sp):
            full = NE // P
            for name, a in zip(NAMES, (etype, src, dst)):
                sp.wait_ge(consts, 1)
                c3 = (COLS // P - 1) * P
                sp.dma_start(raw[name][:, 0:3, :],
                             a[0:c3 * P].rearrange("(c r p) -> r c p", r=P, p=P)).then_inc(raw_in, 16)
                sp.dma_start(raw[name][0:full - c3, 3, :],
                             a[c3 * P:full * P].rearrange("(r p) -> r p", p=P)).then_inc(raw_in, 16)
                sp.dma_start(raw[name][full - c3:full - c3 + 1, 3, 0:NE - full * P],
                             a[full * P:NE].rearrange("(r p) -> r p", r=1)).then_inc(raw_in, 16)
            sp.wait_ge(consts, 2)
            for s in range(2):
                sp.dma_start(agg_halves[s].rearrange("p r f -> p r f"),
                             zeros[:, 0:2 * D].unsqueeze(1).to_broadcast([P, ROWS // (4 * P), 2 * D])
                             ).then_inc(agg_zeroed, 16)
            sp.dma_start(out[SPARE:ROWS, :].rearrange("(p j) d -> p (j d)", j=B), zeros[:, :]).then_inc(spare_set, 16)
            for r in range(R):
                sp.dma_start(w0[:, r, :, :], w_rel[r].rearrange("(c k) d -> k c d", c=KC)).then_inc(weights_in, 16)
            sp.dma_start(w1[:, :, 0:D], w_neigh.rearrange("(c k) d -> k c d", c=KC)).then_inc(weights_in, 16)
            sp.dma_start(w1[:, :, D:2 * D], w_self.rearrange("(c k) d -> k c d", c=KC)).then_inc(weights_in, 16)
            sp.dma_start(bias_sb[:, :], bias.unsqueeze(0).to_broadcast([P, D])).then_inc(weights_in, 16)

            def store_rows(dram, tile, tiles, done):
                whole = tiles // P
                v = dram[0:whole * P * P].rearrange("(c r p) -> r c p", r=P, p=P)
                sp.dma_start(v, tile[:, 0:whole, :]).then_inc(done, 16)
                sp.dma_start(dram[whole * P * P:tiles * P].rearrange("(r p) -> r p", p=P),
                             tile[0:tiles - whole * P, whole, :]).then_inc(done, 16)

            sp.wait_ge(rawf_done, 1)
            store_rows(key1_rows, rawf["dst"], TILES, key1_stored)
            store_rows(low1_rows, lowrow, TILES, key1_stored)
            sp.wait_ge(keyT_done, 1)
            store_rows(key0_rows, rawf["src"], SLOTS, key0_stored)
            sp.wait_ge(key0_stored, 32)

            def load_keys0(b, r, p):
                wait_from(sp, pick0, b - 1, b, 2)
                sp.dma_start(keyrow[p][:, :], key0_rows[bass.ds(b * BE, BE)].unsqueeze(0).to_broadcast([P, BE])
                             ).then_inc(keys0_in[p], 16)

            pipeline(sp, NBT, 2, load_keys0, lambda b, r, p: None)

            edge0_over(sp)

            def load_nodes(b, r, p):
                wait_from(sp, x2_done, b - 1, b, 2)
                last = isinstance(b, int) and b == NB - 1
                parts = (N - (NB - 1) * BE) // B if last else P
                rows = x[(NB - 1) * BE:N, :] if last else x[bass.ds(b * BE, BE), :]
                sp.dma_start(rows_in[p][0:parts, :, :].rearrange("p j d -> p (j d)"),
                             rows.rearrange("(p j) d -> p (j d)", j=B)).then_inc(loaded[p], 16)
                sp.dma_start(agg_in[p][:, :, :].rearrange("p j d -> p (j d)"),
                             agg[bass.ds(b * BE, BE), :].rearrange("(p j) d -> p (j d)", j=B)).then_inc(loaded[p], 16)

            def store_nodes(b, r, p):
                sp.wait_ge(y_n, b + 1)
                sp.dma_start(out[bass.ds(b * BE, BE), :].rearrange("(p j) d -> p (j d)", j=B),
                             msg[p][:, :]).then_inc(y_stored[p], 16)
                sp.wait_ge(top_n, b + 1)
                sp.dma_start(hs[bass.ds(b * BE, BE), :].rearrange("(p j) d -> p (j d)", j=B),
                             top[p][:, :, :].rearrange("p j d -> p (j d)")).then_inc(top_stored[p], 16)

            pipeline(sp, NB, 2, load_nodes, store_nodes)

            node_over(sp)
            sp.wait_ge(key1_stored, 64)

            def load_keys1(b, r, p):
                wait_from(sp, pick1, b - 1, b, 2)
                for tile, rows in ((keyrow, key1_rows), (lowkey, low1_rows)):
                    sp.dma_start(tile[p][:, :], rows[bass.ds(b * BE, BE)].unsqueeze(0).to_broadcast([P, BE])
                                 ).then_inc(keys1_in[p], 16)

            pipeline(sp, NB, 2, load_keys1, lambda b, r, p: None)
            sp.wait_ge(spare_set, 16)
            for q in range(2):
                sp.wait_ge(added1[q], 16 * B * (NB // 2))

        @block.gpsimd
        def _(pool):
            last = COLS // P - 1
            nc.gpsimd.memset(raw["type"][:, last, :], R)
            nc.gpsimd.memset(raw["src"][:, last, :], 0)
            nc.gpsimd.memset(raw["dst"][:, last, :], N).then_inc(consts, 1)
            nc.gpsimd.memset(zeros[:, :], 0.0).then_inc(consts, 1)
            nc.gpsimd.memset(ident[:, :], 0.0)
            nc.gpsimd.memset(ones[:, :], 1.0)
            nc.gpsimd.memset(before[:, :], 1.0)
            nc.gpsimd.memset(upto[:, :], 1.0)
            nc.gpsimd.memset(eps[:, :], EPS)
            for q in range(2):
                nc.gpsimd.memset(rows_in[q][:, :, :], 0.0)
            nc.gpsimd.memset(pos[:, :], 0.0).then_inc(consts, 1)
            pool.wait_ge(consts, 3)
            nc.gpsimd.affine_select(out=ident[:, :], in_=ident[:, :], compare_op=ALU.not_equal, fill=1.0,
                                    base=0, pattern=[[-1, P]], channel_multiplier=1)
            nc.gpsimd.affine_select(out=before[:, :], in_=before[:, :], compare_op=ALU.is_ge, fill=0.0,
                                    base=-1, pattern=[[1, P]], channel_multiplier=-1)
            nc.gpsimd.affine_select(out=upto[:, BE - P:BE], in_=upto[:, BE - P:BE], compare_op=ALU.is_ge,
                                    fill=0.0, base=0, pattern=[[-1, P]], channel_multiplier=1)
            nc.gpsimd.iota(part_i[:, :], pattern=[[0, 1]], base=0, channel_multiplier=1)
            nc.gpsimd.iota(spare_i[:, :], pattern=[[P, B]], base=SPARE, channel_multiplier=1)
            nc.gpsimd.iota(iota_i[:, :], pattern=[[1, COLS]], base=0, channel_multiplier=0).then_inc(consts, 1)

            def gather0(b, r, p):
                wait_from(pool, h0, b - 1, b, 2)
                wait_alone(pool, staged0, b + 1)
                for j in range(B):
                    pool.indirect_dma_start(
                        out=rows_in[p][:, j, :], out_offset=None, in_=x[:, :],
                        in_offset=bass.IndirectOffsetOnAxis(ap=gidx[p][:, j:j + 1], axis=0),
                    ).then_inc(gathered0[p], 16)

            def add0(b, r, p):
                pool.wait_ge(msg0, b + 1)
                wait_from(pool, added0[1 - p], 16 * B * (r + p), b, 1)
                wait_alone(pool, sidx0, b + 1)
                for j in range(B):
                    pool.indirect_dma_start(
                        out=agg[:, :], out_offset=bass.IndirectOffsetOnAxis(ap=sidx[p][:, j:j + 1], axis=0),
                        in_=msg[p][:, j * D:(j + 1) * D], in_offset=None, compute_op=ALU.add,
                    ).then_inc(added0[p], 16)

            pool.wait_ge(agg_zeroed, 32)
            pipeline(pool, NBT, 2, gather0, add0)

            edge0_over(pool)
            pool.wait_ge(weights_in, 16 * (R + 3))
            own2 = Steps(pool_own, 2)

            def residual(b, r, p):
                own2.start(b)
                pool.wait_ge(loaded[p], 32 * (r + 1))
                v = own2.mark(nc.gpsimd.tensor_tensor(agg_in[p][:, :, :], agg_in[p][:, :, :],
                                                      bias_sb[:, :].unsqueeze(1).to_broadcast([P, B, D]), ALU.add))
                wait_alone(pool, pool_own, v)
                v = own2.mark(nc.gpsimd.tensor_scalar_max(agg_in[p][:, :, :], agg_in[p][:, :, :], 0.0))
                pool.wait_ge(pool_own, v)
                nc.gpsimd.tensor_tensor(x2[p][:, :, :], rows_in[p][:, :, :], agg_in[p][:, :, :],
                                        ALU.add).then_inc(x2_done, 1)

            def add_self(b, r, p):
                pool.wait_ge(self_n, b + 1)
                wait_from(pool, y_stored[p], 16 * r, b, 2)
                pool.wait_ge(x2_done, b + 1)
                nc.gpsimd.tensor_tensor(msg[p][:, :].rearrange("p (j d) -> p j d", j=B), x2[p][:, :, :],
                                        self_sb[p][:, :, :], ALU.add).then_inc(y_n, 1)

            pipeline(pool, NB, 1, residual, add_self)

            node_over(pool)
            pool.wait_ge(spare_set, 16)

            def gather1(b, r, p):
                wait_from(pool, foldmm, 2 * b - 2, b, 2)
                wait_alone(pool, staged1, b + 1)
                for j in range(B):
                    pool.indirect_dma_start(
                        out=rows_in[p][:, j, :], out_offset=None, in_=hs[:, :],
                        in_offset=bass.IndirectOffsetOnAxis(ap=gidx[p][:, j:j + 1], axis=0),
                    ).then_inc(gathered1[p], 16)

            def add1(b, r, p):
                wait_from(pool, added1[1 - p], 16 * B * (r + p), b, 1)
                pool.wait_ge(msg1, b + 1)
                wait_alone(pool, sidx1, b + 1)
                for j in range(B):
                    pool.indirect_dma_start(
                        out=out[:, :], out_offset=bass.IndirectOffsetOnAxis(ap=sidx[p][:, j:j + 1], axis=0),
                        in_=msg[p][:, j * D:(j + 1) * D], in_offset=None, compute_op=ALU.add,
                    ).then_inc(added1[p], 16)

            pipeline(pool, NB, 2, gather1, add1)

        @block.vector
        def _(dve):
            count = [0]

            def link(ins):
                count[0] += 1
                ins.then_inc(own, 1)
                dve.wait_ge(own, count[0])

            v = nc.vector

            dve.wait_ge(consts, 4)
            v.tensor_copy(iota_f[:, :], iota_i[:, :])
            v.tensor_copy(iota_h[:, :], iota_i[:, :])
            v.tensor_copy(part_f[:, :], part_i[:, :])
            link(v.tensor_copy(spare_f[:, :], spare_i[:, :]))
            dve.wait_ge(raw_in, 16 * 9)
            for n in NAMES:
                link(v.tensor_copy(rawf[n][:, :, :], raw[n][:, :, :]))
            link(v.tensor_scalar(raw["type"][:, :, :], raw["dst"][:, :, :], P - 1, None, ALU.bitwise_and))
            link(v.tensor_copy(lowrow[:, :, :], raw["type"][:, :, :]))
            v.memset(key0[:, SLOTS:COLS], float(N)).then_inc(rawf_done, 1)
            for k, n in enumerate(NAMES):
                dve.wait_ge(pe_done, k + 1)
                link(v.tensor_copy(tab[n][:, :], bank[k][:, :]))
            v.tensor_copy(src_i[:, :], tab["src"][:, :])
            link(v.tensor_copy(dst_i[:, :], tab["dst"][:, :]))
            for whole, table in ((src_i, val[0]), (dst_i, val[1])):
                link(v.tensor_scalar(tmp_i[:, :], whole[:, :], LOW - 1, None, ALU.bitwise_and))
                link(v.tensor_copy(table[:, :], tmp_i[:, :]))
            link(v.tensor_scalar(tmp_i[:, :], src_i[:, :], LOWBITS, None, ALU.arith_shift_right))
            link(v.tensor_scalar(val[2][:, :], tmp_i[:, :], 32.0, 1024.0, ALU.mult, ALU.add))
            link(v.tensor_scalar(tmp_i[:, :], dst_i[:, :], LOWBITS, None, ALU.arith_shift_right))
            link(v.tensor_tensor(val[2][:, :], val[2][:, :], tmp_i[:, :], ALU.add))
            link(v.tensor_scalar(tmp_i[:, :], dst_i[:, :], P - 1, None, ALU.bitwise_and))
            link(v.tensor_copy(node_low[:, :], tmp_i[:, :]))
            link(v.tensor_scalar(tmp_i[:, :], dst_i[:, :], 7, None, ALU.arith_shift_right))
            link(v.tensor_copy(node_high[:, :], tmp_i[:, :]))
            for r in range(R):
                link(v.tensor_scalar(mask[:, :], tab["type"][:, 0:TILES], float(r), None, ALU.is_equal))
                link(v.tensor_tensor_scan(scan[:, r, :], ones[:, 0:TILES], mask[:, :], 0.0, ALU.mult, ALU.add))
                link(v.tensor_copy(tot[:, r:r + 1], scan[:, r, TILES - 1:TILES]))
            v.memset(btype_f[:, :], 0.0).then_inc(dve_ready, 1)
            dve.wait_ge(pe_done, 4)
            before_me, total = bank[3][:, 0:R], bank[4][:, 0:R]
            link(v.tensor_scalar(cnt_i[:, :], total, float(BE - 1), None, ALU.add))
            link(v.tensor_scalar(cnt_i[:, :], cnt_i[:, :], 9, None, ALU.arith_shift_right))
            link(v.tensor_copy(nbat[:, :], cnt_i[:, :]))
            link(v.tensor_tensor_scan(incl[:, :], ones[:, 0:R], nbat[:, :], 0.0, ALU.mult, ALU.add))
            link(v.tensor_tensor(off[:, :], incl[:, :], nbat[:, :], ALU.subtract))
            link(v.scalar_tensor_tensor(off[:, :], off[:, :], float(BE), before_me, ALU.mult, ALU.add))
            for r in range(R):
                link(v.tensor_scalar(mask[:, :], tab["type"][:, 0:TILES], float(r), None, ALU.is_equal))
                link(v.scalar_tensor_tensor(tmp_f[:, 0:TILES], scan[:, r, :], off[:, r:r + 1], mask[:, :],
                                            ALU.add, ALU.mult))
                link(v.tensor_tensor(pos[:, 0:TILES], pos[:, 0:TILES], tmp_f[:, 0:TILES], ALU.add))
            link(v.tensor_scalar(tmp_i[:, :], pos[:, :], -1.0, None, ALU.add))
            link(v.tensor_scalar(src_i[:, :], tmp_i[:, :], P - 1, None, ALU.bitwise_and))
            link(v.tensor_copy(slot_row[:, :], src_i[:, :]))
            link(v.tensor_scalar(tmp_i[:, :], tmp_i[:, :], 7, None, ALU.arith_shift_right))
            link(v.tensor_copy(slot_tile[:, :], tmp_i[:, :]))
            link(v.tensor_copy(src_i[:, :], tab["src"][:, :]))
            for r in range(R - 1):
                link(v.scalar_tensor_tensor(btype_f[:, :], iota_f[0:1, 0:P], incl[0:1, r:r + 1], btype_f[:, :],
                                            ALU.is_ge, ALU.add))
            v.tensor_copy(btype[:, :], btype_f[:, :]).then_inc(btype_done, 1)

            def one_hots(t, r, p):
                wait_from(dve, hot_used, t - 1, t, 2)
                col = bass.ds(t, 1)
                v.tensor_scalar(one_tile[p][:, :], iota_h[:, 0:SLOTS], slot_tile[:, col], None, ALU.is_equal)
                for k in range(3):
                    v.tensor_scalar(one_row[p][:, k, :], iota_h[:, 0:P], slot_row[:, col], val[k][:, col],
                                    ALU.is_equal, ALU.mult)
                v.tensor_scalar(one_low[p][:, :], iota_h[:, 0:P], node_low[:, col], None, ALU.is_equal)
                v.tensor_scalar(one_high[p][:, :], iota_h[:, 0:TILES], node_high[:, col], None,
                                ALU.is_equal).then_inc(hot, 1)

            pipeline(dve, TILES, 2, one_hots, lambda b, r, p: None)

            dve.wait_ge(hot_used, TILES)
            m = [bank[k][:, 0:SLOTS] for k in range(3)]
            s = slice(0, SLOTS)
            link(v.tensor_copy(tmp_i[:, s], m[2]))
            link(v.tensor_scalar(dst_i[:, s], tmp_i[:, s], 31, None, ALU.bitwise_and))
            link(v.tensor_copy(tmp_f[:, s], dst_i[:, s]))
            v.memset(from0[:, SLOTS:COLS], 0)
            link(v.scalar_tensor_tensor(from0[:, s], tmp_f[:, s], float(LOW), m[1], ALU.mult, ALU.add))
            link(v.tensor_scalar(dst_i[:, s], tmp_i[:, s], 1023, 5, ALU.bitwise_and, ALU.arith_shift_right))
            link(v.tensor_copy(tmp_f[:, s], dst_i[:, s]))
            link(v.scalar_tensor_tensor(key0[:, s], tmp_f[:, s], float(LOW), m[0], ALU.mult, ALU.add))
            link(v.tensor_scalar(tmp_f[:, s], m[2], 0.5, float(N), ALU.is_lt, ALU.mult))
            link(v.tensor_tensor(key0[:, s], key0[:, s], tmp_f[:, s], ALU.add))
            t_ = slice(0, TILES)
            link(v.tensor_copy(tmp_i[:, t_], bank[3][:, t_]))
            link(v.tensor_scalar(dst_i[:, t_], tmp_i[:, t_], LOW - 1, None, ALU.bitwise_and))
            link(v.tensor_copy(deg_lo[:, :], dst_i[:, t_]))
            link(v.tensor_tensor(deg_hi[:, :], tmp_i[:, t_], deg_lo[:, :], ALU.subtract))
            v.tensor_copy(tmp_f[:, 0:1], key0[:, 0:1]).then_inc(dve_ready, 1)
            dve.wait_ge(pe_done, 5)
            v.tensor_copy(rawf["src"][:, :, :], bank[4][:, :].rearrange("p (c q) -> p c q", q=P)
                          ).then_inc(keyT_done, 1)

            def picks(p, done):
                for j in reversed(range(B)):
                    last = v.scalar_tensor_tensor(pick[p][j][:, :], keyrow[p][:, 0:(j + 1) * P],
                                                  keycol[p][:, j:j + 1], upto[:, (B - 1 - j) * P:BE],
                                                  ALU.is_equal, ALU.mult, accum_out=seen[p][:, j:j + 1])
                last.then_inc(done, 1)

            def targets(b, p, picked, extra_sem, done):
                dve.wait_ge(picked, b + 1)
                v.scalar_tensor_tensor(extra[p][:, :], seen[p][:, :], 1.5, spare_f[:, :], ALU.is_gt,
                                       ALU.mult).then_inc(extra_sem, 1)
                dve.wait_ge(extra_sem, b + 1)
                v.tensor_tensor(sidx[p][:, :], extra[p][:, :], keycol[p][:, :], ALU.max).then_inc(done, 1)

            def statistics(b, p, source, stats_sem, var_sem):
                for j in range(B):
                    last = v.bn_stats(stats[p][:, j, :], source[p][:, j, :])
                last.then_inc(stats_sem, 1)
                wait_alone(dve, stats_sem, b + 1)
                for j in range(B):
                    last = v.bn_aggr(mv[p][:, j, :], stats[p][:, j, :])
                last.then_inc(var_sem, 1)

            def scales(b, p, std_sem, recip_sem, done):
                dve.wait_ge(std_sem, b + 1)
                v.reciprocal(rstd[p][:, :], std[p][:, :]).then_inc(recip_sem, 1)
                dve.wait_ge(recip_sem, b + 1)
                v.scalar_tensor_tensor(shift[p][:, :], mv[p][:, :, 0], -1.0, rstd[p][:, :], ALU.mult,
                                       ALU.mult).then_inc(done, 1)

            for b in range(2):
                v.tensor_copy(gidx[b][:, :], from0[:, b * B:(b + 1) * B]).then_inc(staged0, 1)

            def edge0_front(b, r, p):
                dve.wait_ge(gathered0[p], 16 * B * (r + 1))
                v.tensor_copy(gidx[p][:, :], from0[:, bass.ds(b * B + 2 * B, B)]).then_inc(staged0, 1)
                wait_from(dve, sidx0, b - 1, b, 2)
                v.tensor_copy(keycol[p][:, :], key0[:, bass.ds(b * B, B)]).then_inc(col0, 1)
                statistics(b, p, rows_in, stats0, var0)
                dve.wait_ge(keys0_in[p], 16 * (r + 1))
                dve.wait_ge(col0, b + 1)
                picks(p, pick0)
                scales(b, p, std0, recip0, rstd0)

            def edge0_back(b, r, p):
                dve.wait_ge(hTmm0, b + 1)
                for c in range(KC):
                    last = v.tensor_copy(hT[p][:, c, :], bank[KC * p + c][:, :])
                last.then_inc(hT0, 1)
                wait_from(dve, added0[p], 16 * B * r, b, 2)
                targets(b, p, pick0, extra0, sidx0)

            pipeline(dve, NBT, 1, edge0_front, edge0_back)

            edge0_over(dve)
            steps = Steps(topk_own, 2 * (TOPK // 8) * 2)

            def node_front(b, r, p):
                dve.wait_ge(x2_done, b + 1)
                statistics(b, p, x2, stats_n, var_n)
                scales(b, p, std_n, recip_n, rstd_n)

            def node_top(b, r, p):
                halves = [range(0, B // 2), range(B // 2, B)]
                ready = [None, None]
                steps.start(b)
                for k in range(TOPK // 8):
                    for half in range(2):
                        if k == 0:
                            wait_alone(dve, neigh_n, b * B + (half + 1) * (B // 2))
                        else:
                            wait_alone(dve, topk_own, ready[half])
                        for j in halves[half]:
                            last = v.max(best[:, j, :], (work if k else neigh[p])[:, j, :])
                        ready[half] = steps.mark(last)
                    for half in range(2):
                        wait_alone(dve, topk_own, ready[half])
                        for j in halves[half]:
                            last = v.match_replace(work[:, j, :], best[:, j, :],
                                                   (work if k else neigh[p])[:, j, :], NEG)
                        ready[half] = steps.mark(last)
                wait_from(dve, top_stored[p], 16 * r, b, 2)
                for half in range(2):
                    dve.wait_ge(topk_own, ready[half])
                    for j in halves[half]:
                        last = v.scalar_tensor_tensor(top[p][:, j, :], work[:, j, :], NEG, neigh[p][:, j, :],
                                                      ALU.is_equal, ALU.mult)
                last.then_inc(top_n, 1)

            pipeline(dve, NB, 1, node_front, node_top)

            node_over(dve)
            for b in range(2):
                v.tensor_copy(gidx[b][:, :], src_i[:, b * B:(b + 1) * B]).then_inc(staged1, 1)
            degs = Steps(deg_own, 2)

            def edge1_front(b, r, p):
                wait_from(dve, sidx1, b - 1, b, 2)
                v.tensor_copy(highcol[p][:, :], node_high[:, bass.ds(b * B, B)])
                v.tensor_copy(keycol[p][:, :], tab["dst"][:, bass.ds(b * B, B)]).then_inc(col1, 1)
                dve.wait_ge(keys1_in[p], 32 * (r + 1))
                wait_from(dve, foldmm, 2 * b - 2, b, 2)
                v.tensor_scalar(lowT[p][:, :], lowkey[p][:, :], part_f[:, 0:1], None, ALU.is_equal)
                dve.wait_ge(col1, b + 1)
                picks(p, pick1)

            def edge1_back(b, r, p):
                dve.wait_ge(gathered1[p], 16 * B * (r + 1))
                v.tensor_copy(gidx[p][:, :], src_i[:, bass.ds(b * B + 2 * B, B)]).then_inc(staged1, 1)
                dve.wait_ge(degmm, b + 1)
                degs.start(b)
                for j in range(B):
                    last = v.scalar_tensor_tensor(junk[:, j, :], iota_f[:, 0:TILES], highcol[p][:, j:j + 1],
                                                  bank[j][:, 0:TILES], ALU.is_equal, ALU.mult,
                                                  accum_out=deg[p][:, j:j + 1])
                dve.wait_ge(deg_own, degs.mark(last))
                dve.wait_ge(deg_own, degs.mark(v.tensor_scalar_max(deg[p][:, :], deg[p][:, :], 1.0)))
                wait_from(dve, msg1, b - 1, b, 2)
                v.reciprocal(rstd[p][:, :], deg[p][:, :]).then_inc(rdeg1, 1)
                wait_from(dve, added1[p], 16 * B * r, b, 2)
                targets(b, p, pick1, extra1, sidx1)

            pipeline(dve, NB, 1, edge1_front, edge1_back)

        @block.scalar
        def _(act):
            def normalise(b, p, source, var_sem, std_sem, rstd_sem, done):
                act.wait_ge(var_sem, b + 1)
                nc.scalar.activation(std[p][:, :], mv[p][:, :, 1], ACT.Sqrt, bias=eps[:, 0:1]).then_inc(std_sem, 1)
                act.wait_ge(rstd_sem, b + 1)
                for j in range(B):
                    last = nc.scalar.activation(h[p][:, j, :], source[p][:, j, :], ACT.Relu,
                                                bias=shift[p][:, j:j + 1], scale=rstd[p][:, j:j + 1])
                last.then_inc(done, 1)

            def edge0_front(b, r, p):
                normalise(b, p, rows_in, var0, std0, rstd0, h0)

            def edge0_back(b, r, p):
                wait_from(act, added0[p], 16 * B * r, b, 2)
                for half in range(2):
                    act.wait_ge(msgmm0, 2 * b + half + 1)
                    last = nc.scalar.copy(msg[p][:, half * 512:(half + 1) * 512], bank[4 + 2 * p + half][:, :])
                last.then_inc(msg0, 1)

            pipeline(act, NBT, 1, edge0_front, edge0_back)

            edge0_over(act)

            def node_front(b, r, p):
                normalise(b, p, x2, var_n, std_n, rstd_n, h_n)

            def node_back(b, r, p):
                wait_from(act, top_n, b - 1, b, 2)
                wait_from(act, y_n, b - 1, b, 2)
                for j in range(B):
                    act.wait_ge(mm_n, b * B + j + 1)
                    nc.scalar.copy(neigh[p][:, j, :], bank[4 + j][:, 0:D]).then_inc(neigh_n, 1)
                    last = nc.scalar.copy(self_sb[p][:, j, :], bank[4 + j][:, D:2 * D])
                last.then_inc(self_n, 1)

            def node_turned(b, r, p):
                act.wait_ge(hTtr, b + 1)
                for c in range(KC):
                    last = nc.scalar.copy(hT[p][:, c, :], bank[KC * p + c][:, :])
                last.then_inc(hT_n, 1)

            def node_head(b, r, p):
                node_front(b, r, p)
                node_turned(b, r, p)

            pipeline(act, NB, 1, node_head, node_back)

            node_over(act)

            def edge1_back(b, r, p):
                wait_from(act, added1[p], 16 * B * r, b, 2)
                act.wait_ge(rdeg1, b + 1)
                for j in range(B):
                    if j % 2 == 0:
                        act.wait_ge(foldmm, 2 * b + j // 2 + 1)
                    last = nc.scalar.activation(msg[p][:, j * D:(j + 1) * D],
                                                bank[4 + 2 * p + j // 2][:, (j % 2) * D:(j % 2 + 1) * D],
                                                ACT.Copy, scale=rstd[p][:, j:j + 1])
                last.then_inc(msg1, 1)

            pipeline(act, NB, 1, lambda b, r, p: None, edge1_back)

        @block.tensor
        def _(pe):
            mm = nc.tensor.matmul

            pe.wait_ge(consts, 4)
            pe.wait_ge(rawf_done, 1)
            for k, n in enumerate(NAMES):
                for c in range(COLS // P):
                    last = nc.tensor.transpose(bank[k][:, c * P:(c + 1) * P], rawf[n][:, c, :], ident[:, :])
                last.then_inc(pe_done, 1)
            pe.wait_ge(dve_ready, 1)
            mm(bank[3][:, 0:R], before[:, :], tot[:, :], start=True, stop=True)
            mm(bank[4][:, 0:R], ones[:, 0:P], tot[:, :], start=True, stop=True).then_inc(pe_done, 1)

            def collect(t, r, p):
                first = isinstance(t, int) and t == 0
                final = isinstance(t, int) and t == TILES - 1
                pe.wait_ge(hot, t + 1)
                for k in range(3):
                    mm(bank[k][:, 0:SLOTS], one_row[p][:, k, :], one_tile[p][:, :], start=first, stop=final)
                mm(bank[3][:, 0:TILES], one_low[p][:, :], one_high[p][:, :], start=first,
                   stop=final).then_inc(hot_used, 1)

            pipeline(pe, TILES, 2, collect, lambda b, r, p: None)
            pe.wait_ge(dve_ready, 2)
            for c in range(COLS // P):
                last = nc.tensor.transpose(bank[4][:, c * P:(c + 1) * P], key0[:, c * P:(c + 1) * P], ident[:, :])
            last.then_inc(pe_done, 1)

            pe.wait_ge(weights_in, 16 * (R + 3))
            pe.wait_ge(btype_done, 1)
            pe.wait_ge(keyT_done, 1)

            def edge0_fold(b, r, p):
                pe.wait_ge(h0, b + 1)
                pe.wait_ge(pick0, b + 1)
                for c in range(KC):
                    for j in reversed(range(B)):
                        last = mm(bank[KC * p + c][:, 0:(j + 1) * P], h[p][:, j, c * P:(c + 1) * P],
                                  pick[p][j][:, :], start=(j == B - 1), stop=(j == 0))
                last.then_inc(hTmm0, 1)

            def edge0_product(b, r, p):
                rel = nc.tensor.value_load(btype[0:1, bass.ds(b, 1)], min_val=0, max_val=R - 1)
                pe.wait_ge(hT0, b + 1)
                for j in range(B):
                    for c in range(KC):
                        last = mm(bank[4 + 2 * p + j // 2][:, (j % 2) * D:(j % 2 + 1) * D],
                                  hT[p][:, c, j * P:(j + 1) * P],
                                  w0[:, bass.ds(rel, 1), c, :].rearrange("k r d -> k (r d)"),
                                  start=(c == 0), stop=(c == KC - 1))
                    if j % 2:
                        last.then_inc(msgmm0, 1)

            pipeline(pe, NBT, 1, edge0_fold, edge0_product)

            edge0_over(pe)

            def node_turn(b, r, p):
                pe.wait_ge(h_n, b + 1)
                for c in range(KC):
                    for j in range(B):
                        last = nc.tensor.transpose(bank[KC * p + c][:, j * P:(j + 1) * P],
                                                   h[p][:, j, c * P:(c + 1) * P], ident[:, :])
                last.then_inc(hTtr, 1)

            def node_product(b, r, p):
                pe.wait_ge(hT_n, b + 1)
                wait_from(pe, self_n, b, b, 1)
                for j in range(B):
                    for c in range(KC):
                        last = mm(bank[4 + j][:, :], hT[p][:, c, j * P:(j + 1) * P], w1[:, c, :],
                                  start=(c == 0), stop=(c == KC - 1))
                    last.then_inc(mm_n, 1)

            pipeline(pe, NB, 1, node_turn, node_product)

            node_over(pe)

            def edge1_degree(b, r, p):
                pe.wait_ge(pick1, b + 1)
                wait_from(pe, rdeg1, b, b, 1)
                for j in range(B):
                    mm(bank[j][:, 0:TILES], lowT[p][:, j * P:(j + 1) * P], deg_lo[:, :], start=True, stop=False)
                    last = mm(bank[j][:, 0:TILES], lowT[p][:, j * P:(j + 1) * P], deg_hi[:, :], start=False,
                              stop=True)
                last.then_inc(degmm, 1)

            def edge1_fold(b, r, p):
                pe.wait_ge(gathered1[p], 16 * B * (r + 1))
                wait_from(pe, msg1, b - 1, b, 2)
                for i in range(B):
                    for j in range(i, B):
                        last = mm(bank[4 + 2 * p + i // 2][:, (i % 2) * D:(i % 2 + 1) * D],
                                  pick[p][j][:, i * P:(i + 1) * P], rows_in[p][:, j, :],
                                  start=(j == i), stop=(j == B - 1))
                    if i % 2:
                        last.then_inc(foldmm, 1)

            pipeline(pe, NB, 1, edge1_degree, edge1_fold)


_INS = ["x", "src", "dst", "edge_type_8", "L0_gnn_weight", "L0_gnn_bias", "L1_gnn_W_self", "L1_gnn_W_neigh"]


def kernel(**inputs):
    import numpy as _np
    import concourse.bacc as _bacc
    from concourse import mybir as _mybir
    from concourse.bass_utils import run_bass_kernel_spmd as _run

    nc = _bacc.Bacc("TRN2", target_bir_lowering=False, num_devices=1)
    arrays, args = {}, []
    for name in _INS:
        a = _np.ascontiguousarray(inputs[name])
        arrays[f"in_{name}"] = a
        args.append(nc.dram_tensor(f"in_{name}", a.shape, _mybir.dt.from_np(a.dtype), kind="ExternalInput").ap())
    args.append(nc.dram_tensor("out_rows", (ROWS, D), F32, kind="ExternalOutput").ap())
    graph_layers(nc, *args)
    r = _run(nc, [arrays], core_ids=[0])
    return r.results[0]["out_rows"][:N]
```

```python
import concourse.bass as bass
from concourse import mybir
from contextlib import ExitStack

F32 = mybir.dt.float32
F16 = mybir.dt.float16
I32 = mybir.dt.int32
ALU = mybir.AluOpType
ACT = mybir.ActivationFunctionType

P = 128
D = 256
KC = D // P
N = 50000
NE = 50000
R = 8
TOPK = 32
B = 4
BE = B * P
TILES = 392
NB = TILES // B
NBT = 106
SLOTS = NBT * B
COLS = 512
NPAD = TILES * P
SPARE = NPAD
ROWS = NPAD + BE
LOW = 2048
LOWBITS = 11
EPS = 1e-5
NEG = -3.0e38

assert TILES * P >= N and (NE + R * (BE - 1)) // BE <= NBT and NB % 2 == 0 and NBT % 2 == 0


def pipeline(eng, nb, *parts):
    deepest = max(lag for _, lag in parts)
    first, last = 2 + deepest, nb - 3 + deepest % 2

    def step(i, t):
        for part, lag in parts:
            b = t - lag
            if i is not None:
                part(i * 2 + b, i + b // 2, b % 2)
            elif 0 <= b < nb:
                part(b, b // 2, b % 2)

    for t in range(first):
        step(None, t)
    with eng.Fori(0, (last + 1 - first) // 2) as i:
        step(i, first)
        step(i, first + 1)
    for t in range(last + 1, nb + deepest):
        step(None, t)


def wait_from(eng, sem, value, batch, first):
    if not isinstance(batch, int) or batch >= first:
        eng.wait_ge(sem, value)


class Steps:

    def __init__(self, sem, per):
        self.sem, self.per = sem, per

    def start(self, batch):
        self.base, self.k = batch * self.per, 0

    def mark(self, ins):
        ins.then_inc(self.sem, 1)
        self.k += 1
        assert self.k <= self.per
        return self.base + self.k


def graph_layers(nc, x, src, dst, etype, w_rel, bias, w_self, w_neigh, out):
    agg = nc.dram_tensor("agg", [ROWS, D], F32).ap()
    hs = nc.dram_tensor("hs", [NPAD, D], F32).ap()
    key0_rows = nc.dram_tensor("key0_rows", [SLOTS * P], F32).ap()
    key1_rows = nc.dram_tensor("key1_rows", [NPAD], F32).ap()
    low1_rows = nc.dram_tensor("low1_rows", [NPAD], F32).ap()

    ctx = ExitStack()
    with ctx:
        def sb(name, shape, dt=F32):
            return ctx.enter_context(nc.sbuf_tensor(name, shape, dt))

        def sem(name):
            return ctx.enter_context(nc.semaphore(name))

        def pair(name):
            return [sem(f"{name}_even"), sem(f"{name}_odd")]

        bank = [ctx.enter_context(nc.psum_tensor(f"bank{i}", [P, 512], F32)) for i in range(8)]

        iota_i = sb("iota_i", [P, COLS], I32)
        iota_f = sb("iota_f", [P, COLS])
        iota_h = sb("iota_h", [P, COLS], F16)
        part_i = sb("part_i", [P, 1], I32)
        part_f = sb("part_f", [P, 1])
        spare_i = sb("spare_i", [P, B], I32)
        spare_f = sb("spare_f", [P, B])
        ident = sb("ident", [P, P])
        ones = sb("ones", [P, COLS])
        before = sb("before", [P, P])
        upto = sb("upto", [P, BE])
        eps = sb("eps", [P, 1])
        bias2 = sb("bias2", [P, 2, D])
        w0 = sb("w0", [P, R, KC, D])
        w1 = sb("w1", [P, KC, 2 * D])

        NAMES = ("type", "src", "dst")
        raw = {n: sb(f"raw_{n}", [P, COLS // P, P], I32) for n in NAMES}
        rawf = {n: sb(f"rawf_{n}", [P, COLS // P, P]) for n in NAMES}
        tab = {n: sb(f"tab_{n}", [P, COLS]) for n in NAMES}
        lowrow = sb("lowrow", [P, COLS // P, P])
        src_i = sb("src_i", [P, COLS], I32)
        dst_i = sb("dst_i", [P, COLS], I32)
        tmp_i = sb("tmp_i", [P, COLS], I32)
        tmp_f = sb("tmp_f", [P, COLS])
        SLOT_TILE, SLOT_ROW, LOW7, HIGH7, VALUES, FIELDS = 0, 1, 2, 3, 4, 7
        fields = sb("fields", [P, COLS, FIELDS])

        def field(k):
            return fields[:, :, k]

        LOW_HIGH = slice(2, 4)
        node_high = sb("node_high", [P, COLS])
        scan = sb("scan", [P, R, TILES])
        mask = sb("mask", [P, TILES])
        pos = sb("pos", [P, COLS])
        tot = sb("tot", [P, R])
        cnt_i = sb("cnt_i", [P, R], I32)
        nbat = sb("nbat", [P, R])
        incl = sb("incl", [P, R])
        off = sb("off", [P, R])
        btype_f = sb("btype_f", [1, P])
        btype = sb("btype", [1, P], I32)
        key0 = sb("key0", [P, COLS])
        from0 = sb("from0", [P, COLS], I32)
        deg_lo = sb("deg_lo", [P, TILES], F16)
        deg_hi = sb("deg_hi", [P, TILES], F16)

        def two(name, shape, dt=F32):
            return [sb(f"{name}{p}", shape, dt) for p in range(2)]

        rows_in = two("rows_in", [P, B, D])
        h = two("h", [P, B, D])
        hT = two("hT", [P, KC, BE])
        msg = two("msg", [P, B * D])
        pick = [[sb(f"pick{p}{j}", [P, (j + 1) * P]) for j in range(B)] for p in range(2)]
        keyrow = two("keyrow", [P, BE])
        lowkey = two("lowkey", [P, BE])
        lowT = two("lowT", [P, BE], F16)
        gidx = two("gidx", [P, B], I32)
        sidx = two("sidx", [P, B], I32)
        keycol = two("keycol", [P, B])
        highcol = two("highcol", [P, B])
        seen = two("seen", [P, B])
        extra = two("extra", [P, B])
        stats = two("stats", [P, B, 6])
        mv = two("mv", [P, B, 2])
        std = two("std", [P, B])
        rstd = two("rstd", [P, B])
        shift = two("shift", [P, B])
        deg = two("deg", [P, B])
        minus_mean = two("minus_mean", [P, B])
        total_n = two("total_n", [P, B])
        squares = two("squares", [P, B])
        act_junk = sb("act_junk", [P, B, D])
        agg_in = two("agg_in", [P, B, D])
        x2 = two("x2", [P, B, D])
        self_sb = two("self_sb", [P, B, D])
        neigh = two("neigh", [P, B, D])
        top = two("top", [P, B, D])
        lowhigh = two("lowhigh", [P, B, 2])
        fields4 = two("fields4", [P, B, FIELDS])
        one_tile, one_high, one_row, one_low = ([t[:, :, :].bitcast(F16) for t in pair_]
                                                for pair_ in (x2, neigh, h, top))
        work = sb("work", [P, B, D])
        best = sb("best", [P, B, 8])
        junk = scan

        consts = sem("consts")
        raw_in = sem("raw_in")
        weights_in = sem("weights_in")
        own = sem("own")
        dve_ready = sem("dve_ready")
        pe_done = sem("pe_done")
        rawf_done = sem("rawf_done")
        key1_stored = sem("key1_stored")
        fields_done = sem("fields_done")
        row_hot = sem("row_hot")
        values_hot = sem("values_hot")
        hot = sem("hot")
        hot_used = sem("hot_used")
        keyT_done = sem("keyT_done")
        key0_stored = sem("key0_stored")
        btype_done = sem("btype_done")
        gathered0 = pair("gathered0")
        bias_in = sem("bias_in")
        agg_set = sem("agg_set")
        added0 = pair("added0")
        keys0_in = pair("keys0_in")
        staged0 = sem("staged0")
        node_hot = sem("node_hot")
        degrees0 = sem("degrees0")
        stats0 = sem("stats0")
        var0 = sem("var0")
        std0 = sem("std0")
        recip0 = sem("recip0")
        rstd0 = sem("rstd0")
        col0 = sem("col0")
        h0 = sem("h0")
        pick0 = sem("pick0")
        hTmm0 = sem("hTmm0")
        hT0 = sem("hT0")
        msgmm0 = sem("msgmm0")
        msg0 = sem("msg0")
        extra0 = sem("extra0")
        sidx0 = sem("sidx0")
        loaded = pair("loaded")
        relu_n = sem("relu_n")
        x2_done = sem("x2_done")
        sum_n = sem("sum_n")
        mean_n = sem("mean_n")
        var_n = sem("var_n")
        std_n = sem("std_n")
        recip_n = sem("recip_n")
        rstd_n = sem("rstd_n")
        h_n = sem("h_n")
        hTtr = sem("hTtr")
        hT_n = sem("hT_n")
        mm_n = sem("mm_n")
        neigh_n = sem("neigh_n")
        self_n = sem("self_n")
        topk_own = sem("topk_own")
        top_n = sem("top_n")
        y_n = sem("y_n")
        y_stored = pair("y_stored")
        top_stored = pair("top_stored")
        spare_set = sem("spare_set")
        gathered1 = pair("gathered1")
        added1 = pair("added1")
        keys1_in = pair("keys1_in")
        staged1 = sem("staged1")
        col1 = sem("col1")
        pick1 = sem("pick1")
        degmm = sem("degmm")
        deg_own = sem("deg_own")
        rdeg1 = sem("rdeg1")
        foldmm = sem("foldmm")
        msg1 = sem("msg1")
        extra1 = sem("extra1")
        sidx1 = sem("sidx1")

        DEG = 2
        agg_halves = agg.rearrange("(s p r f) d -> s p r (f d)", s=2, p=P, f=2)

        passed = sem("passed")

        def wait_alone(eng, sem, value):
            eng.wait_ge(sem, value)
            eng.sem_inc(passed, 1)

        def edge0_over(eng):
            for q in range(2):
                eng.wait_ge(added0[q], 16 * B * (NBT // 2))

        def node_over(eng):
            for q in range(2):
                eng.wait_ge(y_stored[q], 16 * (NB // 2))
                eng.wait_ge(top_stored[q], 16 * (NB // 2))

        block = ctx.enter_context(nc.Block())

        @block.sync
        def _(sp):
            full = NE // P
            for name, a in zip(NAMES, (etype, src, dst)):
                sp.wait_ge(consts, 1)
                c3 = (COLS // P - 1) * P
                sp.dma_start(raw[name][:, 0:3, :],
                             a[0:c3 * P].rearrange("(c r p) -> r c p", r=P, p=P)).then_inc(raw_in, 16)
                sp.dma_start(raw[name][0:full - c3, 3, :],
                             a[c3 * P:full * P].rearrange("(r p) -> r p", p=P)).then_inc(raw_in, 16)
                sp.dma_start(raw[name][full - c3:full - c3 + 1, 3, 0:NE - full * P],
                             a[full * P:NE].rearrange("(r p) -> r p", r=1)).then_inc(raw_in, 16)
            for k in range(2):
                sp.dma_start(bias2[:, k, :], bias.unsqueeze(0).to_broadcast([P, D])).then_inc(bias_in, 16)
            sp.wait_ge(bias_in, 32)
            bias2_row = bias2[:, :, :].rearrange("p k d -> p (k d)")
            for s in range(2):
                sp.dma_start(agg_halves[s], bias2_row.unsqueeze(1).to_broadcast([P, ROWS // (4 * P), 2 * D])
                             ).then_inc(agg_set, 16)
                sp.dma_start(out[SPARE + s * BE // 2:SPARE + (s + 1) * BE // 2, :].rearrange("(p k) d -> p (k d)", k=2),
                             bias2_row).then_inc(spare_set, 16)
            for r in range(R):
                sp.dma_start(w0[:, r, :, :], w_rel[r].rearrange("(c k) d -> k c d", c=KC)).then_inc(weights_in, 16)
            sp.dma_start(w1[:, :, 0:D], w_neigh.rearrange("(c k) d -> k c d", c=KC)).then_inc(weights_in, 16)
            sp.dma_start(w1[:, :, D:2 * D], w_self.rearrange("(c k) d -> k c d", c=KC)).then_inc(weights_in, 16)

            def store_rows(dram, tile, tiles, done):
                whole = tiles // P
                v = dram[0:whole * P * P].rearrange("(c r p) -> r c p", r=P, p=P)
                sp.dma_start(v, tile[:, 0:whole, :]).then_inc(done, 16)
                sp.dma_start(dram[whole * P * P:tiles * P].rearrange("(r p) -> r p", p=P),
                             tile[0:tiles - whole * P, whole, :]).then_inc(done, 16)

            sp.wait_ge(rawf_done, 1)
            store_rows(key1_rows, rawf["dst"], TILES, key1_stored)
            store_rows(low1_rows, lowrow, TILES, key1_stored)
            sp.wait_ge(keyT_done, 1)
            store_rows(key0_rows, rawf["src"], SLOTS, key0_stored)
            sp.wait_ge(key0_stored, 32)

            def load_keys0(b, r, p):
                wait_from(sp, pick0, b - 1, b, 2)
                sp.dma_start(keyrow[p][:, :], key0_rows[bass.ds(b * BE, BE)].unsqueeze(0).to_broadcast([P, BE])
                             ).then_inc(keys0_in[p], 16)

            pipeline(sp, NBT, (load_keys0, 0))

            edge0_over(sp)

            def load_nodes(b, r, p):
                wait_from(sp, x2_done, b - 1, b, 2)
                last = isinstance(b, int) and b == NB - 1
                parts = (N - (NB - 1) * BE) // B if last else P
                rows = x[(NB - 1) * BE:N, :] if last else x[bass.ds(b * BE, BE), :]
                sp.dma_start(rows_in[p][0:parts, :, :].rearrange("p j d -> p (j d)"),
                             rows.rearrange("(p j) d -> p (j d)", j=B)).then_inc(loaded[p], 16)
                sp.dma_start(agg_in[p][:, :, :].rearrange("p j d -> p (j d)"),
                             agg[bass.ds(b * BE, BE), :].rearrange("(p j) d -> p (j d)", j=B)).then_inc(loaded[p], 16)

            def store_y(b, r, p):
                sp.wait_ge(y_n, b + 1)
                sp.dma_start(out[bass.ds(b * BE, BE), :].rearrange("(p j) d -> p (j d)", j=B),
                             self_sb[p][:, :, :].rearrange("p j d -> p (j d)")).then_inc(y_stored[p], 16)

            def store_top(b, r, p):
                sp.wait_ge(top_n, b + 1)
                sp.dma_start(hs[bass.ds(b * BE, BE), :].rearrange("(p j) d -> p (j d)", j=B),
                             top[p][:, :, :].rearrange("p j d -> p (j d)")).then_inc(top_stored[p], 16)

            pipeline(sp, NB, (load_nodes, 0), (store_y, 3), (store_top, 4))

            node_over(sp)
            sp.wait_ge(key1_stored, 64)

            def load_keys1(b, r, p):
                wait_from(sp, pick1, b - 1, b, 2)
                for tile, rows in ((keyrow, key1_rows), (lowkey, low1_rows)):
                    sp.dma_start(tile[p][:, :], rows[bass.ds(b * BE, BE)].unsqueeze(0).to_broadcast([P, BE])
                                 ).then_inc(keys1_in[p], 16)

            pipeline(sp, NB, (load_keys1, 0))
            sp.wait_ge(spare_set, 32)
            for q in range(2):
                sp.wait_ge(added1[q], 16 * B * (NB // 2))

        @block.gpsimd
        def _(pool):
            last = COLS // P - 1
            nc.gpsimd.memset(raw["type"][:, last, :], R)
            nc.gpsimd.memset(raw["src"][:, last, :], 0)
            nc.gpsimd.memset(raw["dst"][:, last, :], N).then_inc(consts, 1)
            nc.gpsimd.memset(ident[:, :], 0.0)
            nc.gpsimd.memset(ones[:, :], 1.0)
            nc.gpsimd.memset(before[:, :], 1.0)
            nc.gpsimd.memset(upto[:, :], 1.0)
            nc.gpsimd.memset(eps[:, :], EPS)
            for q in range(2):
                nc.gpsimd.memset(rows_in[q][:, :, :], 0.0)
            nc.gpsimd.memset(pos[:, :], 0.0).then_inc(consts, 1)
            pool.wait_ge(consts, 2)
            nc.gpsimd.affine_select(out=ident[:, :], in_=ident[:, :], compare_op=ALU.not_equal, fill=1.0,
                                    base=0, pattern=[[-1, P]], channel_multiplier=1)
            nc.gpsimd.affine_select(out=before[:, :], in_=before[:, :], compare_op=ALU.is_ge, fill=0.0,
                                    base=-1, pattern=[[1, P]], channel_multiplier=-1)
            nc.gpsimd.affine_select(out=upto[:, BE - P:BE], in_=upto[:, BE - P:BE], compare_op=ALU.is_ge,
                                    fill=0.0, base=0, pattern=[[-1, P]], channel_multiplier=1)
            nc.gpsimd.iota(part_i[:, :], pattern=[[0, 1]], base=0, channel_multiplier=1)
            nc.gpsimd.iota(spare_i[:, :], pattern=[[P, B]], base=SPARE, channel_multiplier=1)
            nc.gpsimd.iota(iota_i[:, :], pattern=[[1, COLS]], base=0, channel_multiplier=0).then_inc(consts, 1)

            def gather0(b, r, p):
                wait_from(pool, h0, b - 1, b, 2)
                wait_alone(pool, staged0, b + 1)
                for j in range(B):
                    pool.indirect_dma_start(
                        out=rows_in[p][:, j, :], out_offset=None, in_=x[:, :],
                        in_offset=bass.IndirectOffsetOnAxis(ap=gidx[p][:, j:j + 1], axis=0),
                    ).then_inc(gathered0[p], 16)

            def add0(b, r, p):
                pool.wait_ge(msg0, b + 1)
                wait_from(pool, added0[1 - p], 16 * B * (r + p), b, 1)
                wait_alone(pool, sidx0, b + 1)
                for j in range(B):
                    pool.indirect_dma_start(
                        out=agg[:, :], out_offset=bass.IndirectOffsetOnAxis(ap=sidx[p][:, j:j + 1], axis=0),
                        in_=msg[p][:, j * D:(j + 1) * D], in_offset=None, compute_op=ALU.add,
                    ).then_inc(added0[p], 16)

            pool.wait_ge(agg_set, 32)
            pipeline(pool, NBT, (gather0, 0), (add0, 3))

            edge0_over(pool)

            def relu_agg(b, r, p):
                wait_alone(pool, loaded[p], 32 * (r + 1))
                nc.gpsimd.tensor_scalar_max(agg_in[p][:, :, :], agg_in[p][:, :, :], 0.0).then_inc(relu_n, 1)

            def residual(b, r, p):
                wait_from(pool, h_n, b - 1, b, 2)
                pool.wait_ge(relu_n, b + 1)
                nc.gpsimd.tensor_tensor(x2[p][:, :, :], rows_in[p][:, :, :], agg_in[p][:, :, :],
                                        ALU.add).then_inc(x2_done, 1)

            def add_self(b, r, p):
                pool.wait_ge(self_n, b + 1)
                pool.wait_ge(sum_n, b + 1)
                nc.gpsimd.tensor_tensor(self_sb[p][:, :, :], msg[p][:, :].rearrange("p (j d) -> p j d", j=B),
                                        self_sb[p][:, :, :], ALU.add).then_inc(y_n, 1)

            pipeline(pool, NB, (relu_agg, 0), (residual, 0), (add_self, 2))

            node_over(pool)
            pool.wait_ge(spare_set, 32)

            def gather1(b, r, p):
                wait_from(pool, foldmm, 2 * b - 2, b, 2)
                wait_alone(pool, staged1, b + 1)
                for j in range(B):
                    pool.indirect_dma_start(
                        out=rows_in[p][:, j, :], out_offset=None, in_=hs[:, :],
                        in_offset=bass.IndirectOffsetOnAxis(ap=gidx[p][:, j:j + 1], axis=0),
                    ).then_inc(gathered1[p], 16)

            def add1(b, r, p):
                wait_from(pool, added1[1 - p], 16 * B * (r + p), b, 1)
                pool.wait_ge(msg1, b + 1)
                wait_alone(pool, sidx1, b + 1)
                for j in range(B):
                    pool.indirect_dma_start(
                        out=out[:, :], out_offset=bass.IndirectOffsetOnAxis(ap=sidx[p][:, j:j + 1], axis=0),
                        in_=msg[p][:, j * D:(j + 1) * D], in_offset=None, compute_op=ALU.add,
                    ).then_inc(added1[p], 16)

            pipeline(pool, NB, (gather1, 0), (add1, 3))

        @block.vector
        def _(dve):
            count = [0]

            def link(ins):
                count[0] += 1
                ins.then_inc(own, 1)
                dve.wait_ge(own, count[0])

            v = nc.vector

            dve.wait_ge(consts, 3)
            v.tensor_copy(iota_f[:, :], iota_i[:, :])
            v.tensor_copy(iota_h[:, :], iota_i[:, :])
            v.tensor_copy(part_f[:, :], part_i[:, :])
            link(v.tensor_copy(spare_f[:, :], spare_i[:, :]))
            dve.wait_ge(raw_in, 16 * 9)
            for n in NAMES:
                link(v.tensor_copy(rawf[n][:, :, :], raw[n][:, :, :]))
            link(v.tensor_scalar(raw["type"][:, :, :], raw["dst"][:, :, :], P - 1, None, ALU.bitwise_and))
            link(v.tensor_copy(lowrow[:, :, :], raw["type"][:, :, :]))
            v.memset(key0[:, SLOTS:COLS], float(N)).then_inc(rawf_done, 1)
            for k, n in enumerate(NAMES):
                dve.wait_ge(pe_done, k + 1)
                link(v.tensor_copy(tab[n][:, :], bank[k][:, :]))
            v.tensor_copy(src_i[:, :], tab["src"][:, :])
            link(v.tensor_copy(dst_i[:, :], tab["dst"][:, :]))
            for whole, table in ((src_i, field(VALUES)), (dst_i, field(VALUES + 1))):
                link(v.tensor_scalar(tmp_i[:, :], whole[:, :], LOW - 1, None, ALU.bitwise_and))
                link(v.tensor_copy(table, tmp_i[:, :]))
            high_parts = field(VALUES + 2)
            link(v.tensor_scalar(tmp_i[:, :], src_i[:, :], LOWBITS, None, ALU.arith_shift_right))
            link(v.tensor_scalar(high_parts, tmp_i[:, :], 32.0, 1024.0, ALU.mult, ALU.add))
            link(v.tensor_scalar(tmp_i[:, :], dst_i[:, :], LOWBITS, None, ALU.arith_shift_right))
            link(v.tensor_tensor(high_parts, high_parts, tmp_i[:, :], ALU.add))
            link(v.tensor_scalar(tmp_i[:, :], dst_i[:, :], P - 1, None, ALU.bitwise_and))
            link(v.tensor_copy(field(LOW7), tmp_i[:, :]))
            link(v.tensor_scalar(tmp_i[:, :], dst_i[:, :], 7, None, ALU.arith_shift_right))
            v.tensor_copy(field(HIGH7), tmp_i[:, :])
            link(v.tensor_copy(node_high[:, :], tmp_i[:, :]))
            for r in range(R):
                link(v.tensor_scalar(mask[:, :], tab["type"][:, 0:TILES], float(r), None, ALU.is_equal))
                link(v.tensor_tensor_scan(scan[:, r, :], ones[:, 0:TILES], mask[:, :], 0.0, ALU.mult, ALU.add))
                link(v.tensor_copy(tot[:, r:r + 1], scan[:, r, TILES - 1:TILES]))
            v.memset(btype_f[:, :], 0.0).then_inc(dve_ready, 1)
            dve.wait_ge(pe_done, 4)
            before_me, total = bank[3][:, 0:R], bank[4][:, 0:R]
            link(v.tensor_scalar(cnt_i[:, :], total, float(BE - 1), None, ALU.add))
            link(v.tensor_scalar(cnt_i[:, :], cnt_i[:, :], 9, None, ALU.arith_shift_right))
            link(v.tensor_copy(nbat[:, :], cnt_i[:, :]))
            link(v.tensor_tensor_scan(incl[:, :], ones[:, 0:R], nbat[:, :], 0.0, ALU.mult, ALU.add))
            link(v.tensor_tensor(off[:, :], incl[:, :], nbat[:, :], ALU.subtract))
            link(v.scalar_tensor_tensor(off[:, :], off[:, :], float(BE), before_me, ALU.mult, ALU.add))
            for r in range(R):
                link(v.tensor_scalar(mask[:, :], tab["type"][:, 0:TILES], float(r), None, ALU.is_equal))
                link(v.scalar_tensor_tensor(tmp_f[:, 0:TILES], scan[:, r, :], off[:, r:r + 1], mask[:, :],
                                            ALU.add, ALU.mult))
                link(v.tensor_tensor(pos[:, 0:TILES], pos[:, 0:TILES], tmp_f[:, 0:TILES], ALU.add))
            link(v.tensor_scalar(tmp_i[:, :], pos[:, :], -1.0, None, ALU.add))
            link(v.tensor_scalar(src_i[:, :], tmp_i[:, :], P - 1, None, ALU.bitwise_and))
            link(v.tensor_copy(field(SLOT_ROW), src_i[:, :]))
            link(v.tensor_scalar(tmp_i[:, :], tmp_i[:, :], 7, None, ALU.arith_shift_right))
            link(v.tensor_copy(field(SLOT_TILE), tmp_i[:, :]))
            link(v.tensor_copy(src_i[:, :], tab["src"][:, :]))
            for r in range(R - 1):
                link(v.scalar_tensor_tensor(btype_f[:, :], iota_f[0:1, 0:P], incl[0:1, r:r + 1], btype_f[:, :],
                                            ALU.is_ge, ALU.add))
            v.tensor_copy(btype[:, :], btype_f[:, :]).then_inc(btype_done, 1)

            def one_hots(b, r, p):
                wait_from(dve, hot_used, b - 1, b, 2)
                v.tensor_copy(fields4[p][:, :, :], fields[:, bass.ds(b * B, B), :]).then_inc(fields_done, 1)
                dve.wait_ge(fields_done, b + 1)
                for j in range(B):
                    f = [fields4[p][:, j, k:k + 1] for k in range(FIELDS)]
                    v.tensor_scalar(one_low[p][:, j, 0:P], iota_h[:, 0:P], f[SLOT_ROW], None,
                                    ALU.is_equal).then_inc(row_hot, 1)
                    v.tensor_scalar(one_row[p][:, j, 0:P], iota_h[:, 0:P], f[SLOT_ROW], f[VALUES], ALU.is_equal,
                                    ALU.mult)
                    last = v.tensor_scalar(one_tile[p][:, j, 0:SLOTS], iota_h[:, 0:SLOTS], f[SLOT_TILE], None,
                                           ALU.is_equal)
                last.then_inc(hot, 1)

            pipeline(dve, NB, (one_hots, 0))

            dve.wait_ge(hot_used, NB)
            m = [bank[k][:, 0:SLOTS] for k in range(3)]
            s = slice(0, SLOTS)
            link(v.tensor_copy(tmp_i[:, s], m[2]))
            link(v.tensor_scalar(dst_i[:, s], tmp_i[:, s], 31, None, ALU.bitwise_and))
            link(v.tensor_copy(tmp_f[:, s], dst_i[:, s]))
            v.memset(from0[:, SLOTS:COLS], 0)
            link(v.scalar_tensor_tensor(from0[:, s], tmp_f[:, s], float(LOW), m[1], ALU.mult, ALU.add))
            link(v.tensor_scalar(dst_i[:, s], tmp_i[:, s], 1023, 5, ALU.bitwise_and, ALU.arith_shift_right))
            link(v.tensor_copy(tmp_f[:, s], dst_i[:, s]))
            link(v.scalar_tensor_tensor(key0[:, s], tmp_f[:, s], float(LOW), m[0], ALU.mult, ALU.add))
            link(v.tensor_scalar(tmp_f[:, s], m[2], 0.5, float(N), ALU.is_lt, ALU.mult))
            link(v.tensor_tensor(key0[:, s], key0[:, s], tmp_f[:, s], ALU.add))
            v.tensor_copy(tmp_f[:, 0:1], key0[:, 0:1]).then_inc(dve_ready, 1)
            dve.wait_ge(pe_done, 5)
            v.tensor_copy(rawf["src"][:, :, :], bank[4][:, :].rearrange("p (c q) -> p c q", q=P)
                          ).then_inc(keyT_done, 1)

            def picks(p, done):
                for j in reversed(range(B)):
                    last = v.scalar_tensor_tensor(pick[p][j][:, :], keyrow[p][:, 0:(j + 1) * P],
                                                  keycol[p][:, j:j + 1], upto[:, (B - 1 - j) * P:BE],
                                                  ALU.is_equal, ALU.mult, accum_out=seen[p][:, j:j + 1])
                last.then_inc(done, 1)

            def targets(b, p, picked, extra_sem, done):
                dve.wait_ge(picked, b + 1)
                v.scalar_tensor_tensor(extra[p][:, :], seen[p][:, :], 1.5, spare_f[:, :], ALU.is_gt,
                                       ALU.mult).then_inc(extra_sem, 1)
                dve.wait_ge(extra_sem, b + 1)
                v.tensor_tensor(sidx[p][:, :], extra[p][:, :], keycol[p][:, :], ALU.max).then_inc(done, 1)

            def statistics(b, p, source, stats_sem, var_sem):
                for j in range(B):
                    last = v.bn_stats(stats[p][:, j, :], source[p][:, j, :])
                last.then_inc(stats_sem, 1)
                wait_alone(dve, stats_sem, b + 1)
                for j in range(B):
                    last = v.bn_aggr(mv[p][:, j, :], stats[p][:, j, :])
                last.then_inc(var_sem, 1)

            def scales(b, p, std_sem, recip_sem, done):
                dve.wait_ge(std_sem, b + 1)
                v.reciprocal(rstd[p][:, :], std[p][:, :]).then_inc(recip_sem, 1)
                dve.wait_ge(recip_sem, b + 1)
                v.scalar_tensor_tensor(shift[p][:, :], mv[p][:, :, 0], -1.0, rstd[p][:, :], ALU.mult,
                                       ALU.mult).then_inc(done, 1)

            for b in range(2):
                v.tensor_copy(gidx[b][:, :], from0[:, b * B:(b + 1) * B]).then_inc(staged0, 1)

            def edge0_front(b, r, p):
                wait_from(dve, sidx0, b - 1, b, 2)
                v.tensor_copy(lowhigh[p][:, :, :], fields[:, bass.ds(b * B, B), LOW_HIGH])
                v.tensor_copy(keycol[p][:, :], key0[:, bass.ds(b * B, B)]).then_inc(col0, 1)
                wait_from(dve, hTmm0, b - 1, b, 2)
                dve.wait_ge(keys0_in[p], 16 * (r + 1))
                dve.wait_ge(col0, b + 1)
                picks(p, pick0)
                wait_from(dve, degrees0, b - 1, b, 2)
                for j in range(B):
                    v.tensor_scalar(one_low[p][:, j, 0:P], iota_h[:, 0:P], lowhigh[p][:, j, 0:1], None, ALU.is_equal)
                    last = v.tensor_scalar(one_high[p][:, j, 0:TILES], iota_h[:, 0:TILES], lowhigh[p][:, j, 1:2],
                                           None, ALU.is_equal)
                last.then_inc(node_hot, 1)
                dve.wait_ge(gathered0[p], 16 * B * (r + 1))
                v.tensor_copy(gidx[p][:, :], from0[:, bass.ds(b * B + 2 * B, B)]).then_inc(staged0, 1)
                statistics(b, p, rows_in, stats0, var0)
                scales(b, p, std0, recip0, rstd0)

            def edge0_back(b, r, p):
                wait_from(dve, added0[p], 16 * B * r, b, 2)
                targets(b, p, pick0, extra0, sidx0)

            pipeline(dve, NBT, (edge0_back, 2), (edge0_front, 0))

            edge0_over(dve)
            dve.wait_ge(degrees0, NBT)
            t_ = slice(0, TILES)
            link(v.tensor_copy(tmp_i[:, t_], bank[DEG][:, t_]))
            link(v.tensor_scalar(dst_i[:, t_], tmp_i[:, t_], LOW - 1, None, ALU.bitwise_and))
            link(v.tensor_copy(deg_lo[:, :], dst_i[:, t_]))
            link(v.tensor_tensor(deg_hi[:, :], tmp_i[:, t_], deg_lo[:, :], ALU.subtract))
            steps = Steps(topk_own, 2 * (TOPK // 8) * 2)

            def node_front(b, r, p):
                dve.wait_ge(std_n, b + 1)
                v.reciprocal(rstd[p][:, :], std[p][:, :]).then_inc(recip_n, 1)
                dve.wait_ge(recip_n, b + 1)
                v.tensor_tensor(shift[p][:, :], minus_mean[p][:, :], rstd[p][:, :], ALU.mult).then_inc(rstd_n, 1)

            def node_top(b, r, p):
                halves = [range(0, B // 2), range(B // 2, B)]
                ready = [None, None]
                steps.start(b)
                for k in range(TOPK // 8):
                    for half in range(2):
                        if k == 0:
                            wait_alone(dve, neigh_n, b + 1)
                        else:
                            wait_alone(dve, topk_own, ready[half])
                        for j in halves[half]:
                            last = v.max(best[:, j, :], (work if k else neigh[p])[:, j, :])
                        ready[half] = steps.mark(last)
                    for half in range(2):
                        wait_alone(dve, topk_own, ready[half])
                        for j in halves[half]:
                            last = v.match_replace(work[:, j, :], best[:, j, :],
                                                   (work if k else neigh[p])[:, j, :], NEG)
                        ready[half] = steps.mark(last)
                wait_from(dve, top_stored[p], 16 * r, b, 2)
                for half in range(2):
                    dve.wait_ge(topk_own, ready[half])
                    for j in halves[half]:
                        last = v.scalar_tensor_tensor(top[p][:, j, :], work[:, j, :], NEG, neigh[p][:, j, :],
                                                      ALU.is_equal, ALU.mult)
                last.then_inc(top_n, 1)

            pipeline(dve, NB, (node_front, 0), (node_top, 2))

            node_over(dve)
            for b in range(2):
                v.tensor_copy(gidx[b][:, :], src_i[:, b * B:(b + 1) * B]).then_inc(staged1, 1)
            degs = Steps(deg_own, 2)

            def edge1_front(b, r, p):
                wait_from(dve, sidx1, b - 1, b, 2)
                v.tensor_copy(highcol[p][:, :], node_high[:, bass.ds(b * B, B)])
                v.tensor_copy(keycol[p][:, :], tab["dst"][:, bass.ds(b * B, B)]).then_inc(col1, 1)
                dve.wait_ge(keys1_in[p], 32 * (r + 1))
                wait_from(dve, foldmm, 2 * b - 2, b, 2)
                v.tensor_scalar(lowT[p][:, :], lowkey[p][:, :], part_f[:, 0:1], None, ALU.is_equal)
                dve.wait_ge(col1, b + 1)
                picks(p, pick1)

            def edge1_back(b, r, p):
                dve.wait_ge(gathered1[p], 16 * B * (r + 1))
                v.tensor_copy(gidx[p][:, :], src_i[:, bass.ds(b * B + 2 * B, B)]).then_inc(staged1, 1)
                dve.wait_ge(degmm, b + 1)
                degs.start(b)
                for j in range(B):
                    last = v.scalar_tensor_tensor(junk[:, j, :], iota_f[:, 0:TILES], highcol[p][:, j:j + 1],
                                                  bank[j][:, 0:TILES], ALU.is_equal, ALU.mult,
                                                  accum_out=deg[p][:, j:j + 1])
                dve.wait_ge(deg_own, degs.mark(last))
                dve.wait_ge(deg_own, degs.mark(v.tensor_scalar_max(deg[p][:, :], deg[p][:, :], 1.0)))
                wait_from(dve, msg1, b - 1, b, 2)
                v.reciprocal(rstd[p][:, :], deg[p][:, :]).then_inc(rdeg1, 1)
                wait_from(dve, added1[p], 16 * B * r, b, 2)
                targets(b, p, pick1, extra1, sidx1)

            pipeline(dve, NB, (edge1_front, 0), (edge1_back, 1))

        @block.scalar
        def _(act):
            def value_rows(b, r, p):
                wait_from(act, hot_used, b - 1, b, 2)
                for j in range(B):
                    act.wait_ge(row_hot, b * B + j + 1)
                    for k in range(1, 3):
                        last = nc.scalar.activation(one_row[p][:, j, k * P:(k + 1) * P], one_low[p][:, j, 0:P],
                                                    ACT.Copy, scale=fields4[p][:, j, VALUES + k:VALUES + k + 1])
                last.then_inc(values_hot, 1)

            pipeline(act, NB, (value_rows, 0))

            def normalise(b, p, source, rstd_sem, done):
                act.wait_ge(rstd_sem, b + 1)
                for j in range(B):
                    last = nc.scalar.activation(h[p][:, j, :], source[p][:, j, :], ACT.Relu,
                                                bias=shift[p][:, j:j + 1], scale=rstd[p][:, j:j + 1])
                last.then_inc(done, 1)

            def edge0_front(b, r, p):
                act.wait_ge(var0, b + 1)
                nc.scalar.activation(std[p][:, :], mv[p][:, :, 1], ACT.Sqrt, bias=eps[:, 0:1]).then_inc(std0, 1)
                normalise(b, p, rows_in, rstd0, h0)

            def edge0_turned(b, r, p):
                wait_from(act, msgmm0, 2 * b - 2, b, 2)
                act.wait_ge(hTmm0, b + 1)
                for c in range(KC):
                    last = nc.scalar.copy(hT[p][:, c, :], bank[c][:, :])
                last.then_inc(hT0, 1)

            def edge0_back(b, r, p):
                wait_from(act, added0[p], 16 * B * r, b, 2)
                for half in range(2):
                    act.wait_ge(msgmm0, 2 * b + half + 1)
                    last = nc.scalar.copy(msg[p][:, half * 512:(half + 1) * 512], bank[4 + 2 * p + half][:, :])
                last.then_inc(msg0, 1)

            pipeline(act, NBT, (edge0_turned, 1), (edge0_front, 0), (edge0_back, 2))

            edge0_over(act)

            def node_stats(b, r, p):
                act.wait_ge(x2_done, b + 1)
                wait_from(act, y_n, b - 1, b, 2)
                for j in range(B):
                    last = nc.scalar.activation(msg[p][:, j * D:(j + 1) * D], x2[p][:, j, :], ACT.Copy,
                                                accum_out=total_n[p][:, j:j + 1])
                last.then_inc(sum_n, 1)
                act.wait_ge(sum_n, b + 1)
                nc.scalar.mul(minus_mean[p][:, :], total_n[p][:, :], -1.0 / D).then_inc(mean_n, 1)
                act.wait_ge(mean_n, b + 1)
                for j in range(B):
                    last = nc.scalar.activation(act_junk[:, j, :], x2[p][:, j, :], ACT.Square,
                                                bias=minus_mean[p][:, j:j + 1],
                                                accum_out=squares[p][:, j:j + 1])
                last.then_inc(var_n, 1)
                act.wait_ge(var_n, b + 1)
                nc.scalar.activation(std[p][:, :], squares[p][:, :], ACT.Sqrt, bias=eps[:, 0:1],
                                     scale=1.0 / D).then_inc(std_n, 1)

            def node_front(b, r, p):
                normalise(b, p, x2, rstd_n, h_n)

            def node_self(b, r, p):
                wait_from(act, y_stored[p], 16 * r, b, 2)
                for j in range(B):
                    act.wait_ge(mm_n, b * B + j + 1)
                    last = nc.scalar.copy(self_sb[p][:, j, :], bank[4 + j][:, D:2 * D])
                last.then_inc(self_n, 1)

            def node_neigh(b, r, p):
                wait_from(act, top_n, b - 1, b, 2)
                for j in range(B):
                    last = nc.scalar.copy(neigh[p][:, j, :], bank[4 + j][:, 0:D])
                last.then_inc(neigh_n, 1)

            def node_turned(b, r, p):
                act.wait_ge(hTtr, b + 1)
                for c in range(KC):
                    last = nc.scalar.copy(hT[p][:, c, :], bank[KC * p + c][:, :])
                last.then_inc(hT_n, 1)

            pipeline(act, NB, (node_front, 1), (node_self, 2), (node_neigh, 2), (node_turned, 1), (node_stats, 0))

            node_over(act)

            def edge1_back(b, r, p):
                wait_from(act, added1[p], 16 * B * r, b, 2)
                act.wait_ge(rdeg1, b + 1)
                for j in range(B):
                    if j % 2 == 0:
                        act.wait_ge(foldmm, 2 * b + j // 2 + 1)
                    last = nc.scalar.activation(msg[p][:, j * D:(j + 1) * D],
                                                bank[4 + 2 * p + j // 2][:, (j % 2) * D:(j % 2 + 1) * D],
                                                ACT.Copy, scale=rstd[p][:, j:j + 1])
                last.then_inc(msg1, 1)

            pipeline(act, NB, (edge1_back, 0))

        @block.tensor
        def _(pe):
            mm = nc.tensor.matmul

            pe.wait_ge(consts, 3)
            pe.wait_ge(rawf_done, 1)
            for k, n in enumerate(NAMES):
                for c in range(COLS // P):
                    last = nc.tensor.transpose(bank[k][:, c * P:(c + 1) * P], rawf[n][:, c, :], ident[:, :])
                last.then_inc(pe_done, 1)
            pe.wait_ge(dve_ready, 1)
            mm(bank[3][:, 0:R], before[:, :], tot[:, :], start=True, stop=True)
            mm(bank[4][:, 0:R], ones[:, 0:P], tot[:, :], start=True, stop=True).then_inc(pe_done, 1)

            def collect(b, r, p):
                pe.wait_ge(hot, b + 1)
                pe.wait_ge(values_hot, b + 1)
                for j in range(B):
                    first = isinstance(b, int) and b == 0 and j == 0
                    final = isinstance(b, int) and b == NB - 1 and j == B - 1
                    for k in range(3):
                        last = mm(bank[k][:, 0:SLOTS], one_row[p][:, j, k * P:(k + 1) * P], one_tile[p][:, j, 0:SLOTS],
                           start=first, stop=final)
                last.then_inc(hot_used, 1)

            pipeline(pe, NB, (collect, 0))
            pe.wait_ge(dve_ready, 2)
            for c in range(COLS // P):
                last = nc.tensor.transpose(bank[4][:, c * P:(c + 1) * P], key0[:, c * P:(c + 1) * P], ident[:, :])
            last.then_inc(pe_done, 1)

            pe.wait_ge(weights_in, 16 * (R + 2))
            pe.wait_ge(btype_done, 1)
            pe.wait_ge(keyT_done, 1)

            def edge0_fold(b, r, p):
                pe.wait_ge(h0, b + 1)
                pe.wait_ge(pick0, b + 1)
                wait_from(pe, hT0, b, b, 1)
                for c in range(KC):
                    for j in reversed(range(B)):
                        last = mm(bank[c][:, 0:(j + 1) * P], h[p][:, j, c * P:(c + 1) * P],
                                  pick[p][j][:, :], start=(j == B - 1), stop=(j == 0))
                last.then_inc(hTmm0, 1)
                pe.wait_ge(node_hot, b + 1)
                for j in range(B):
                    last = mm(bank[DEG][:, 0:TILES], one_low[p][:, j, 0:P], one_high[p][:, j, 0:TILES],
                              start=isinstance(b, int) and b == 0 and j == 0,
                              stop=isinstance(b, int) and b == NBT - 1 and j == B - 1)
                last.then_inc(degrees0, 1)

            def edge0_product(b, r, p):
                rel = nc.tensor.value_load(btype[0:1, bass.ds(b, 1)], min_val=0, max_val=R - 1)
                wait_from(pe, msg0, b - 1, b, 2)
                pe.wait_ge(hT0, b + 1)
                for j in range(B):
                    for c in range(KC):
                        last = mm(bank[4 + 2 * p + j // 2][:, (j % 2) * D:(j % 2 + 1) * D],
                                  hT[p][:, c, j * P:(j + 1) * P],
                                  w0[:, bass.ds(rel, 1), c, :].rearrange("k r d -> k (r d)"),
                                  start=(c == 0), stop=(c == KC - 1))
                    if j % 2:
                        last.then_inc(msgmm0, 1)

            pipeline(pe, NBT, (edge0_fold, 0), (edge0_product, 1))

            edge0_over(pe)

            def node_turn(b, r, p):
                pe.wait_ge(h_n, b + 1)
                for c in range(KC):
                    for j in range(B):
                        last = nc.tensor.transpose(bank[KC * p + c][:, j * P:(j + 1) * P],
                                                   h[p][:, j, c * P:(c + 1) * P], ident[:, :])
                last.then_inc(hTtr, 1)

            def node_product(b, r, p):
                pe.wait_ge(hT_n, b + 1)
                wait_from(pe, neigh_n, b, b, 1)
                for j in range(B):
                    for c in range(KC):
                        last = mm(bank[4 + j][:, :], hT[p][:, c, j * P:(j + 1) * P], w1[:, c, :],
                                  start=(c == 0), stop=(c == KC - 1))
                    last.then_inc(mm_n, 1)

            pipeline(pe, NB, (node_turn, 0), (node_product, 0))

            node_over(pe)

            def edge1_degree(b, r, p):
                pe.wait_ge(pick1, b + 1)
                wait_from(pe, rdeg1, b, b, 1)
                for j in range(B):
                    mm(bank[j][:, 0:TILES], lowT[p][:, j * P:(j + 1) * P], deg_lo[:, :], start=True, stop=False)
                    last = mm(bank[j][:, 0:TILES], lowT[p][:, j * P:(j + 1) * P], deg_hi[:, :], start=False,
                              stop=True)
                last.then_inc(degmm, 1)

            def edge1_fold(b, r, p):
                pe.wait_ge(gathered1[p], 16 * B * (r + 1))
                wait_from(pe, msg1, b - 1, b, 2)
                for i in range(B):
                    for j in range(i, B):
                        last = mm(bank[4 + 2 * p + i // 2][:, (i % 2) * D:(i % 2 + 1) * D],
                                  pick[p][j][:, i * P:(i + 1) * P], rows_in[p][:, j, :],
                                  start=(j == i), stop=(j == B - 1))
                    if i % 2:
                        last.then_inc(foldmm, 1)

            pipeline(pe, NB, (edge1_fold, 1), (edge1_degree, 0))


_INS = ["x", "src", "dst", "edge_type_8", "L0_gnn_weight", "L0_gnn_bias", "L1_gnn_W_self", "L1_gnn_W_neigh"]


def kernel(**inputs):
    import numpy as _np
    import concourse.bacc as _bacc
    from concourse import mybir as _mybir
    from concourse.bass_utils import run_bass_kernel_spmd as _run

    nc = _bacc.Bacc("TRN2", target_bir_lowering=False, num_devices=1)
    arrays, args = {}, []
    for name in _INS:
        a = _np.ascontiguousarray(inputs[name])
        arrays[f"in_{name}"] = a
        args.append(nc.dram_tensor(f"in_{name}", a.shape, _mybir.dt.from_np(a.dtype), kind="ExternalInput").ap())
    args.append(nc.dram_tensor("out_rows", (ROWS, D), F32, kind="ExternalOutput").ap())
    graph_layers(nc, *args)
    r = _run(nc, [arrays], core_ids=[0])
    return r.results[0]["out_rows"][:N]
```
